# Optimizing a Trainium2 kernel written in Bass

```python
import numpy as np
import jax
import jax.numpy as jnp

def _softmax(x, axis=-1):
    return jax.nn.softmax(x, axis=axis)

def _gelu(x):
    return jax.nn.gelu(x, approximate=True)

def _silu(x):
    return jax.nn.silu(x)

def _sigmoid(x):
    return jax.nn.sigmoid(x)

def _layernorm(x, axis=-1, eps=1e-05):
    m = jnp.mean(x, axis=axis, keepdims=True)
    v = jnp.var(x, axis=axis, keepdims=True)
    return (x - m) / jnp.sqrt(v + eps)

def _scatter_add(tgt, idx, src, axis=0):
    return tgt.at[idx].add(src)

def _segment_sum(src, seg, n):
    return jax.ops.segment_sum(src, seg, n)
kernel_name = 'mk_hybrid_d1_jaxref_r8_5ee010'

def setup_inputs(seed: int=0):
    np.random.seed(seed)
    _w = jnp.asarray

    def _L0_attn_a_setup():
        import jax, jax.numpy as jnp
        import numpy as np
        HEADS, DK, DV = (16, 16, 64)
        EPS = 1e-12

        def l2norm(t):
            n = jnp.linalg.norm(t, axis=-1, keepdims=True)
            return t / jnp.maximum(n, EPS)

        def tanh_norm(t):
            n = jnp.linalg.norm(t, axis=-1, keepdims=True)
            return jnp.tanh(n) * (t / jnp.maximum(n, EPS))

        def split_heads(x, h):
            b, n, hd = x.shape
            return x.reshape(b, n, h, hd // h).transpose(0, 2, 1, 3)
        key = jax.random.key(seed)
        k1, k2, k3, k4 = jax.random.split(key, 4)
        b, n, dim = (2, 256, 128)
        tokens = jax.random.normal(k1, (b, n, dim), dtype=jnp.float32)
        Wq = jax.random.normal(k2, (dim, DK * HEADS), dtype=jnp.float32) * 0.02
        Wkv = jax.random.normal(k3, (dim, (DK + DV) * HEADS), dtype=jnp.float32) * 0.02
        Wout = jax.random.normal(k4, (DV * HEADS, dim), dtype=jnp.float32) * 0.02
        return {'tokens': tokens, 'Wq': Wq, 'Wkv': Wkv, 'Wout': Wout}
    _L0_attn_a_in = _L0_attn_a_setup()

    def _L0_attn_b_setup():
        import jax, jax.numpy as jnp
        import numpy as np
        B, L, D = (8, 512, 128)
        K = 32
        key = jax.random.key(seed)
        kx, kw, kb = jax.random.split(key, 3)
        x = jax.random.normal(kx, (B, L, D), dtype=jnp.float32)
        W = jax.random.normal(kw, (K, D), dtype=jnp.float32) * 0.02
        b = jax.random.normal(kb, (K,), dtype=jnp.float32) * 0.02
        return {'x': x, 'W': W, 'b': b}
    _L0_attn_b_in = _L0_attn_b_setup()

    def _L0_ffn_setup():
        import jax, jax.numpy as jnp
        import numpy as np
        B, S, D = (4, 128, 128)
        I = 64
        E = 32
        TOP_K = 8
        N_GROUP = 8
        TOPK_GROUP = 4

        def _group_topk(scores):
            T = scores.shape[0]
            epg = E // N_GROUP
            group_scores = scores.reshape(T, N_GROUP, epg).sum(axis=-1)
            _, top_groups = jax.lax.top_k(group_scores, TOPK_GROUP)
            group_mask = jnp.zeros((T, N_GROUP), scores.dtype).at[jnp.arange(T)[:, None], top_groups].set(1.0)
            expert_mask = jnp.repeat(group_mask, epg, axis=1)
            masked_scores = scores * expert_mask
            topk_w, topk_i = jax.lax.top_k(masked_scores, TOP_K)
            return (topk_w, topk_i)

        def _reference_tuple_inner(hidden_states, gate_w, expert_gate, expert_up, expert_down, shared_gate_w, shared_up_w, shared_down_w):
            b, s, d = hidden_states.shape
            flat = hidden_states.reshape(-1, d)
            T = flat.shape[0]
            logits = flat @ gate_w.T
            scores = jax.nn.sigmoid(logits)
            topk_w, topk_i = _group_topk(scores)
            topk_w = topk_w / jnp.clip(topk_w.sum(axis=-1, keepdims=True), 1e-12)
            combine = jnp.zeros((T, E), flat.dtype).at[jnp.arange(T)[:, None], topk_i].add(topk_w)

            def body(acc, expert):
                wg, wu, wd, w = expert
                h = jax.nn.silu(flat @ wg.T) * (flat @ wu.T)
                return (acc + w[:, None] * (h @ wd.T), None)
            out, _ = jax.lax.scan(body, jnp.zeros_like(flat), (expert_gate, expert_up, expert_down, combine.T))
            shared = jax.nn.silu(flat @ shared_gate_w.T) * (flat @ shared_up_w.T) @ shared_down_w.T
            out = out + shared
            return (out.reshape(b, s, d), logits)
        key = jax.random.key(seed)
        ks = jax.random.split(key, 8)
        scale = 0.02
        return {'hidden_states': jax.random.normal(ks[0], (B, S, D), jnp.float32), 'gate_w': jax.random.normal(ks[1], (E, D), jnp.float32) * scale, 'expert_gate': jax.random.normal(ks[2], (E, I, D), jnp.float32) * scale, 'expert_up': jax.random.normal(ks[3], (E, I, D), jnp.float32) * scale, 'expert_down': jax.random.normal(ks[4], (E, D, I), jnp.float32) * scale, 'shared_gate_w': jax.random.normal(ks[5], (I, D), jnp.float32) * scale, 'shared_up_w': jax.random.normal(ks[6], (I, D), jnp.float32) * scale, 'shared_down_w': jax.random.normal(ks[7], (D, I), jnp.float32) * scale}
    _L0_ffn_in = _L0_ffn_setup()
    _d = {'L0_attn_a_tokens': _L0_attn_a_in['tokens'], 'L0_attn_a_Wq': _L0_attn_a_in['Wq'], 'L0_attn_a_Wkv': _L0_attn_a_in['Wkv'], 'L0_attn_a_Wout': _L0_attn_a_in['Wout'], 'L0_attn_b_W': _L0_attn_b_in['W'], 'L0_attn_b_b': _L0_attn_b_in['b'], 'L0_ffn_gate_w': _L0_ffn_in['gate_w'], 'L0_ffn_expert_gate': _L0_ffn_in['expert_gate'], 'L0_ffn_expert_up': _L0_ffn_in['expert_up'], 'L0_ffn_expert_down': _L0_ffn_in['expert_down'], 'L0_ffn_shared_gate_w': _L0_ffn_in['shared_gate_w'], 'L0_ffn_shared_up_w': _L0_ffn_in['shared_up_w'], 'L0_ffn_shared_down_w': _L0_ffn_in['shared_down_w']}
    _x0 = _d['L0_attn_a_tokens']
    _d['L0_attn_a_tokens'] = jax.random.normal(jax.random.fold_in(jax.random.key(seed), 1), (8, 256, 128), dtype=_x0.dtype)
    del _x0
    return _d

def reference(L0_attn_a_tokens, L0_attn_a_Wq, L0_attn_a_Wkv, L0_attn_a_Wout, L0_attn_b_W, L0_attn_b_b, L0_ffn_gate_w, L0_ffn_expert_gate, L0_ffn_expert_up, L0_ffn_expert_down, L0_ffn_shared_gate_w, L0_ffn_shared_up_w, L0_ffn_shared_down_w):

    def _L0_attn_a_ref(tokens, Wq, Wkv, Wout):
        import jax, jax.numpy as jnp
        import numpy as np
        HEADS, DK, DV = (16, 16, 64)
        EPS = 1e-12

        def l2norm(t):
            n = jnp.linalg.norm(t, axis=-1, keepdims=True)
            return t / jnp.maximum(n, EPS)

        def tanh_norm(t):
            n = jnp.linalg.norm(t, axis=-1, keepdims=True)
            return jnp.tanh(n) * (t / jnp.maximum(n, EPS))

        def split_heads(x, h):
            b, n, hd = x.shape
            return x.reshape(b, n, h, hd // h).transpose(0, 2, 1, 3)
        q = split_heads(tokens @ Wq, HEADS)
        kv = split_heads(tokens @ Wkv, HEADS)
        k, v = (kv[..., :DK], kv[..., DK:])
        q, k, v = (l2norm(q), l2norm(k), l2norm(v))
        sim = jnp.einsum('bhid,bhjd->bhij', q, k)
        attn = jnp.square(jax.nn.relu(sim))
        out = jnp.einsum('bhij,bhjd->bhid', attn, v)
        out = tanh_norm(out)
        b, h, n, d = out.shape
        out = out.transpose(0, 2, 1, 3).reshape(b, n, h * d)
        return out @ Wout

    def _L0_attn_b_ref(x, W, b):
        import jax, jax.numpy as jnp
        import numpy as np
        B, L, D = (8, 512, 128)
        K = 32
        logits = jnp.einsum('bld,kd->blk', x, W) + b
        w = jax.nn.softmax(logits, axis=-1)
        Bn, Ln, Dn = x.shape
        Kn = w.shape[-1]
        xp = jnp.pad(x, ((0, 0), (0, Kn - 1), (0, 0)))
        out = jnp.zeros_like(x)
        for d in range(Kn):
            out = out + w[:, :, d:d + 1] * xp[:, d:d + Ln]
        return out

    def _L0_ffn_ref(hidden_states, gate_w, expert_gate, expert_up, expert_down, shared_gate_w, shared_up_w, shared_down_w):
        import jax, jax.numpy as jnp
        import numpy as np
        B, S, D = (4, 128, 128)
        I = 64
        E = 32
        TOP_K = 8
        N_GROUP = 8
        TOPK_GROUP = 4

        def _group_topk(scores):
            T = scores.shape[0]
            epg = E // N_GROUP
            group_scores = scores.reshape(T, N_GROUP, epg).sum(axis=-1)
            _, top_groups = jax.lax.top_k(group_scores, TOPK_GROUP)
            group_mask = jnp.zeros((T, N_GROUP), scores.dtype).at[jnp.arange(T)[:, None], top_groups].set(1.0)
            expert_mask = jnp.repeat(group_mask, epg, axis=1)
            masked_scores = scores * expert_mask
            topk_w, topk_i = jax.lax.top_k(masked_scores, TOP_K)
            return (topk_w, topk_i)

        def _reference_tuple_inner(hidden_states, gate_w, expert_gate, expert_up, expert_down, shared_gate_w, shared_up_w, shared_down_w):
            b, s, d = hidden_states.shape
            flat = hidden_states.reshape(-1, d)
            T = flat.shape[0]
            logits = flat @ gate_w.T
            scores = jax.nn.sigmoid(logits)
            topk_w, topk_i = _group_topk(scores)
            topk_w = topk_w / jnp.clip(topk_w.sum(axis=-1, keepdims=True), 1e-12)
            combine = jnp.zeros((T, E), flat.dtype).at[jnp.arange(T)[:, None], topk_i].add(topk_w)

            def body(acc, expert):
                wg, wu, wd, w = expert
                h = jax.nn.silu(flat @ wg.T) * (flat @ wu.T)
                return (acc + w[:, None] * (h @ wd.T), None)
            out, _ = jax.lax.scan(body, jnp.zeros_like(flat), (expert_gate, expert_up, expert_down, combine.T))
            shared = jax.nn.silu(flat @ shared_gate_w.T) * (flat @ shared_up_w.T) @ shared_down_w.T
            out = out + shared
            return (out.reshape(b, s, d), logits)
        return _reference_tuple_inner(hidden_states, gate_w, expert_gate, expert_up, expert_down, shared_gate_w, shared_up_w, shared_down_w)[0]
    x = L0_attn_a_tokens
    x = x + _L0_attn_a_ref(_layernorm(x, axis=-1), L0_attn_a_Wq, L0_attn_a_Wkv, L0_attn_a_Wout)
    x = x + _L0_ffn_ref(_layernorm(x, axis=-1), L0_ffn_gate_w, L0_ffn_expert_gate, L0_ffn_expert_up, L0_ffn_expert_down, L0_ffn_shared_gate_w, L0_ffn_shared_up_w, L0_ffn_shared_down_w)
    x = x + _L0_attn_b_ref(_layernorm(x, axis=-1), L0_attn_b_W, L0_attn_b_b)
    x = x + _L0_ffn_ref(_layernorm(x, axis=-1), L0_ffn_gate_w, L0_ffn_expert_gate, L0_ffn_expert_up, L0_ffn_expert_down, L0_ffn_shared_gate_w, L0_ffn_shared_up_w, L0_ffn_shared_down_w)
    return x

_drawn_inputs = setup_inputs


def setup_inputs(seed=0):
    import zlib

    import numpy as np

    out = dict(_drawn_inputs(seed))
    spreads = {}
    factors = {'L0_attn_b_b': 8.0,
     'L0_ffn_gate_w': 8.0,
     'L0_ffn_expert_gate': 8.0,
     'L0_ffn_expert_up': 8.0,
     'L0_ffn_expert_down': 8.0,
     'L0_ffn_shared_gate_w': 7.094,
     'L0_ffn_shared_up_w': 7.057,
     'L0_ffn_shared_down_w': 7.053}
    for name, (base, spread) in spreads.items():
        noise = np.random.default_rng([zlib.crc32(name.encode()), seed]).standard_normal(out[name].shape)
        drawn = base * np.exp(spread * noise) if base else spread * noise
        out[name] = jnp.asarray(drawn.astype(out[name].dtype))
    for name, factor in factors.items():
        out[name] = (out[name] * factor).astype(out[name].dtype)
    return out
```

```python
from contextlib import ExitStack

import numpy as np
import concourse.bass as bass
from concourse import mybir

F32 = mybir.dt.float32
F32R = mybir.dt.float32r
I32 = mybir.dt.int32
ALU = mybir.AluOpType
ACT = mybir.ActivationFunctionType
AX = mybir.AxisListType

P = 128
B, L, D = 8, 256, 128
T = B * L
NT = T // P
H, DK, DV = 16, 16, 64
SLOT = 32
HG = P // SLOT
NG = H // HG
E, I, TOPK, NGRP, TOPG = 32, 64, 8, 8, 4
EPG = E // NGRP
K = 32
CT = 4
CH = CT * P
NC = T // CH
NPAIR = E // 2 + 1
SH = NPAIR - 1
LAG = 3
PAD = CT
LN_EPS = 1e-5
NORM_EPS = 1e-12
BW = P + K
QK = H * DK
WQ_G, WK_G, W_QK, W_V = 0, NG * P, 2 * NG * P, 2 * NG * P + 2 * QK
WA = W_V + H * DV
WG0, WU0, WD0 = 0, NPAIR * P, 2 * NPAIR * P
WF = 3 * NPAIR * P
FS = WF // B


class Sems:

    def __init__(self, ctx, nc, stage, names):
        self.by_name = {n: ctx.enter_context(nc.semaphore(f"{stage}_{n}")) for n in names.split()}
        self.base = {}

    def __call__(self, name):
        return self.by_name[name]

    def count(self, name, n):
        return self.by_name[name], n + self.base.get(name, 0)

    def again(self, totals):
        second = Sems.__new__(Sems)
        second.by_name, second.base = self.by_name, totals
        return second


def after(engine, semaphore, count):
    if isinstance(count, int) and count <= 0:
        return
    engine.wait_ge(semaphore, count)


def wait_apart(engine, constant, semaphore, count):
    if isinstance(count, int):
        return after(engine, semaphore, count)
    count = engine.snap(count)
    engine.compute_val(count)
    engine.wait_ge(constant, 1)
    engine.wait_ge(semaphore, count)


def hybrid_layer(nc, x_in, wa_in, wo_in, wb_in, bb_in, gw_in, eg_in, eu_in, ed_in, sg_in, su_in, sd_in, band, out):
    with ExitStack() as ctx:
        def sb(name, shape, dt=F32):
            return ctx.enter_context(nc.sbuf_tensor(name, shape, dt))

        X = sb("X", [P, (NT + PAD) * D])
        ident = sb("ident", [P, P])
        half = sb("half", [P, 2])
        lowrows = sb("lowrows", [P, 1])
        rowid = sb("rowid", [P, 1], I32)
        rowbit = sb("rowbit", [P, 1], I32)
        negw = sb("negw", [2 * E, 1])
        wout = sb("wout", [P, H * DV // P, D])
        wfh = sb("wfh", [P, WF], F32R)
        wfl = sb("wfl", [P, WF], F32R)
        gw = sb("gw", [P, E])
        wb = sb("wb", [P, K])
        bb = sb("bb", [P, K])
        stats = sb("stats", [P, CT, 6])
        mv = sb("mv", [P, CT, 2])
        ve = sb("ve", [P, CT])
        rstd = sb("rstd", [P, CT])
        xn = sb("xn", [P, CT, P])

        PS = ctx.enter_context(nc.psum_tensor("PS", [P, 8, 512], F32))

        LN = "stats mv ve rstd xn xT "
        ld = Sems(ctx, nc, "in", "x0 x wa wo wb bb gw eg eu ed sg su sd zero")
        cs = Sems(ctx, nc, "const", "id0 id half rid rbit low neg pad fpad dpad sel0 sel1 sel2 sel zero wah wal wf")
        A = Sems(ctx, nc, "att", LN + "xh xl tv tqk qk sqv vraw sqqk qkh n2 nm rr kql vi c v S relu a av "
                 "sqO n2o sr n nmx rec f1 th f op OT OTs y ys yT xnew")
        per_prep = {n: 1 for n in "ve rstd xT x32 xh xl lg sc gs gr gsel ms ws wmx winv wsel cT wh wT".split()}
        per_prep |= {n: CT for n in "stats mv xn g8 gm m8 mr".split()} | {"comb": 2}
        per_chunk = {n: NPAIR for n in "G U silu h hh hl dn".split()} | {"WB": SH, "t": SH}
        per_chunk |= {n: 1 for n in "oT fin xnew".split()}
        F1 = Sems(ctx, nc, "ffn", " ".join(per_prep | per_chunk))
        F2 = F1.again({n: k * (NC + 1) for n, k in per_prep.items()} | {n: k * NC for n, k in per_chunk.items()})
        M = Sems(ctx, nc, "mix", LN + "x32 xb lg lb mx ls e es er w put get bT bs1 bs2 o xnew")
        fin_out = ctx.enter_context(nc.semaphore("out_written"))

        with ExitStack() as att:
            def ab(name, shape, dt=F32):
                return att.enter_context(nc.sbuf_tensor(name, shape, dt))

            wf = ab("wf", [P, WF])
            wa = ab("wa", [P, WA])
            wah = ab("wah", [P, WA], F32R)
            wal = ab("wal", [P, WA], F32R)
            xTh = ab("xTh", [P, L], F32R)
            xTl = ab("xTl", [P, L], F32R)
            sq = ab("sq", [P, 2, 2 * QK + H * DV])
            vraw = ab("vraw", [P, 2, H * DV])
            vp = ab("vp", [P, 2, H * DV])
            n2 = ab("n2", [P, 2, 3 * H])
            nm = ab("nm", [P, 2, 3 * H])
            rr = ab("rr", [P, 2, 2 * H])
            vi = ab("vi", [P, 2, H])
            vc = ab("vc", [P, 2, H])
            qkh = ab("qkh", [P, NG, 2 * L], F32R)
            ql = ab("ql", [P, NG, L], F32R)
            kst = ab("kst", [P, NG, L], F32R)
            rl = ab("rl", [P, 2, 2 * L])
            aT = ab("aT", [P, 4, 2 * L])
            sqO = ab("sqO", [P, 2, 512])
            n2o = ab("n2o", [P, 2, H // 2])
            sr = ab("sr", [P, 2, H // 2])
            nn = ab("nn", [P, 2, H // 2])
            nmx = ab("nmx", [P, 2, H // 2])
            rec = ab("rec", [P, 2, H // 2])
            f1 = ab("f1", [P, 2, H // 2])
            th = ab("th", [P, 2, H // 2])
            ff = ab("ff", [P, 2, H // 2])
            Op = ab("Op", [P, 2, 2, 512])
            OTs = ab("OTs", [P, H * DV // P, L])
            yTs = ab("yTs", [P, L])
        with ExitStack() as rest:
            def rb(name, shape, dt=F32):
                return rest.enter_context(nc.sbuf_tensor(name, shape, dt))

            selr = rb("selr", [2 * E, SH, P], F32R)
            self32 = rb("self32", [2 * E, SH, P])
            zero = rb("zero", [P, BW])
            x32 = rb("x32", [P, CH])
            fxh = rb("fxh", [P, (NC + 1) * CH], F32R)
            fxl = rb("fxl", [P, (NC + 1) * CH], F32R)
            sc = rb("sc", [P, CT * E])
            gs = rb("gs", [P, CT, NGRP + TOPG])
            g8 = rb("g8", [P, CT, 8])
            gr = rb("gr", [P, CT, 8])
            gm = rb("gm", [P, CT, NGRP + TOPG])
            gsel = rb("gsel", [P, CT * NGRP])
            ms = rb("ms", [P, CT, E])
            m8 = rb("m8", [P, CT, 8])
            mr = rb("mr", [P, CT, E])
            ws = rb("ws", [P, CT])
            wmx = rb("wmx", [P, CT])
            winv = rb("winv", [P, CT])
            wsel = rb("wsel", [P, CT, E])
            comb = rb("comb", [P, CT, 2, E])
            wh = rb("wh", [2 * E, CH], F32R)
            wT = rb("wT", [2 * E, (NC + 1) * CH], F32R)
            xnb = rb("xnb", [P, (NC + 1) * CH])
            silu = rb("silu", [P, 2, CH])
            tt = rb("tt", [P, 2, CH])
            hb = rb("hb", [P, 4, CH])
            hh = rb("hh", [P, 4, CH], F32R)
            hl = rb("hl", [P, 4, CH], F32R)
            oT = rb("oT", [P, CH])
            lb = rb("lb", [P, CT, K])
            mx = rb("mx", [P, CT])
            ls = rb("ls", [P, CT, K])
            ee = rb("ee", [P, CT, K])
            es = rb("es", [P, CT])
            er = rb("er", [P, CT])
            wS = rb("wS", [P, (NC + 1) * CT * K])
            band4 = rb("band4", [P, CT, BW])
            bs1 = rb("bs1", [P, CT, P])
            bs2 = rb("bs2", [K, CT // 2, P])

        block = ctx.enter_context(nc.Block())
        ds = bass.ds
        x_tiles = x_in.rearrange("(t p) d -> p t d", p=P)
        out_tiles = out.rearrange("(t p) d -> p t d", p=P)
        band_taps = band.rearrange("t (p q) -> p t q", q=BW + 1)
        band_rows = band[:, 0:P * BW].rearrange("t (p q) -> p t q", q=BW)
        GBANK = [2, 3, 4, 1]

        def Xt(tile, n=1):
            return X[:, ds(tile * D, n * D)]

        def prev(c, p, depth):
            if p >= depth:
                return c, p - depth
            q = max(q for q in range(NPAIR) if q % depth == p % depth)
            return c - 1, q

        @block.sync
        def _(sp):
            sp.dma_start(X[:, 0:CH].rearrange("p (t d) -> p t d", d=D), x_tiles[:, 0:CT, :]).then_inc(ld("x0"), 16)
            sp.dma_start(wa[:, :], wa_in).then_inc(ld("wa"), 16)
            sp.dma_start(X[:, CH:T].rearrange("p (t d) -> p t d", d=D), x_tiles[:, CT:NT, :]).then_inc(ld("x"), 16)
            sp.dma_start(wout[:, :, :], wo_in.rearrange("(k p) d -> p k d", p=P)).then_inc(ld("wo"), 16)
            sp.dma_start(wf[:, WG0:WG0 + E * I], eg_in).then_inc(ld("eg"), 16)
            sp.dma_start(wf[:, WG0 + E * I:WG0 + E * I + I], sg_in).then_inc(ld("sg"), 16)
            sp.dma_start(wf[:, WU0:WU0 + E * I], eu_in).then_inc(ld("eu"), 16)
            sp.dma_start(wf[:, WU0 + E * I:WU0 + E * I + I], su_in).then_inc(ld("su"), 16)
            sp.dma_start(wf[:, WD0:WD0 + SH * P], ed_in).then_inc(ld("ed"), 16)
            sp.dma_start(wf[0:I, WD0 + SH * P:WF], sd_in).then_inc(ld("sd"), 16)
            sp.dma_start(gw[:, :], gw_in).then_inc(ld("gw"), 16)
            sp.dma_start(wb[:, :], wb_in).then_inc(ld("wb"), 16)
            sp.dma_start(bb[:, :], bb_in.partition_broadcast(P)).then_inc(ld("bb"), 16)
            sp.wait_ge(cs("zero"), 1)
            for t in range(NT):
                sp.dma_start(band_rows[:, t, :], zero[:, :]).then_inc(ld("zero"), 16)
            sp.wait_ge(ld("zero"), 16 * NT)
            with sp.Fori(0, NC) as c:
                sp.wait_ge(M("w"), c + 1)
                for t in range(CT):
                    sp.dma_start(band_taps[:, ds(c * CT + t, 1), 0:K],
                                 wS[:, ds((c * CT + t) * K, K)].rearrange("p (o k) -> p o k", o=1)).then_inc(M("put"), 16)
            sp.wait_ge(M("put"), 16 * NT)
            sp.dma_start(band4[:, :, :], band_rows[:, 0:CT, :]).then_inc(M("get"), 16)
            with sp.Fori(1, NC) as c:
                sp.wait_ge(M("bT"), c)
                sp.dma_start(band4[:, :, :], band_rows[:, ds(c * CT, CT), :]).then_inc(M("get"), 16)
            with sp.Fori(0, NC) as c:
                sp.wait_ge(*F2.count("xnew", c + 1))
                sp.dma_start(out_tiles[:, ds(c * CT, CT), :],
                             Xt(c * CT, CT).rearrange("p (t d) -> p t d", d=D)).then_inc(fin_out, 16)
            sp.wait_ge(fin_out, 16 * NC)

        @block.gpsimd
        def _(pool):
            g = nc.gpsimd
            g.memset(ident[:, :], 0.0).then_inc(cs("id0"), 1)
            g.memset(half[:, 0:1], 0.5).then_inc(cs("half"), 1)
            g.memset(half[:, 1:2], -0.5).then_inc(cs("half"), 1)
            g.iota(rowid[:, :], pattern=[[0, 1]], base=0, channel_multiplier=1).then_inc(cs("rid"), 1)
            pool.wait_ge(cs("id0"), 1)
            g.affine_select(out=ident[:, :], in_=ident[:, :], compare_op=ALU.not_equal, fill=1.0, base=0,
                            pattern=[[-1, P]], channel_multiplier=1).then_inc(cs("id"), 1)
            pool.wait_ge(cs("half"), 2)

            def inverse_deviation(S, i, n):
                wait_apart(pool, cs("id0"), *S.count("mv", n * (i + 1)))
                g.tensor_scalar(ve[:, 0:n], mv[:, 0:n, 1], LN_EPS, None, ALU.add).then_inc(S("ve"), 1)
                pool.wait_ge(*S.count("ve", i + 1))
                g.tensor_tensor(rstd[:, 0:n], ve[:, 0:n], half[:, 1:2].to_broadcast([P, n]), ALU.pow).then_inc(S("rstd"), 1)

            inverse_deviation(A, 0, 2)
            g.memset(X[:, T:(NT + PAD) * D], 0.0).then_inc(cs("pad"), 1)
            g.memset(wf[:, WG0 + E * I + I:WU0], 0.0).then_inc(cs("fpad"), 1)
            g.memset(wf[:, WU0 + E * I + I:WD0], 0.0).then_inc(cs("fpad"), 1)

            def head_norms(b, hf):
                pool.wait_ge(A("n2o"), 2 * b + hf + 1)
                g.tensor_tensor(sr[:, :, :], n2o[:, :, :], half[:, 0:1].unsqueeze(2).to_broadcast([P, 2, H // 2]),
                                ALU.pow).then_inc(A("sr"), 1)
                pool.wait_ge(A("sr"), 2 * b + hf + 1)
                g.tensor_tensor(nn[:, :, :], sr[:, :, :], rr[:, :, hf * (H // 2):(hf + 1) * (H // 2)],
                                ALU.mult).then_inc(A("n"), 1)

            def attention(b):
                pool.wait_ge(A("rr"), b + 1)
                g.tensor_tensor(vi[:, :, :], nm[:, :, 2 * H:3 * H], half[:, 1:2].unsqueeze(2).to_broadcast([P, 2, H]),
                                ALU.pow).then_inc(A("vi"), 1)
                pool.wait_ge(A("vi"), b + 1)
                g.tensor_tensor(vc[:, :, :], vi[:, :, :], rr[:, :, H:2 * H], ALU.mult).then_inc(A("c"), 1)
                pool.wait_ge(A("c"), b + 1)
                after(pool, A("av"), H * b)
                for t in range(2):
                    pool.wait_ge(A("vraw"), 2 * b + t + 1)
                    g.tensor_tensor(vp[:, t, :].rearrange("p (h d) -> p h d", d=DV),
                                    vraw[:, t, :].rearrange("p (h d) -> p h d", d=DV),
                                    vc[:, t, :].unsqueeze(2).to_broadcast([P, H, DV]), ALU.mult).then_inc(A("v"), 1)
                inverse_deviation(A, b + 1, 2)
                g.tensor_copy(wfh[:, ds(b * FS, FS)], wf[:, ds(b * FS, FS)]).then_inc(cs("wf"), 1)
                pool.wait_ge(cs("wf"), 2 * b + 1)
                g.tensor_tensor(wfl[:, ds(b * FS, FS)], wf[:, ds(b * FS, FS)], wfh[:, ds(b * FS, FS)].bitcast(F32),
                                ALU.subtract).then_inc(cs("wf"), 1)
                head_norms(b, 0)
                head_norms(b, 1)

            for w in ("eg", "eu", "ed", "sg", "su", "sd"):
                pool.wait_ge(ld(w), 16)
            pool.wait_ge(cs("fpad"), 2)
            pool.wait_ge(cs("dpad"), 1)
            attention(0)
            with pool.Fori(1, B) as b:
                attention(b)

            def prep_low(S, i):
                pool.wait_ge(*S.count("xh", i + 1))
                g.tensor_tensor(fxl[:, ds(i * CH, CH)], x32[:, :], fxh[:, ds(i * CH, CH)].bitcast(F32),
                                ALU.subtract).then_inc(S("xl"), 1)

            def experts(S, c):
                for p in range(NPAIR):
                    n = c * NPAIR + p
                    pool.wait_ge(*S.count("hh", n + 1))
                    pc, q = prev(c, p, 4)
                    after(pool, *S.count("dn", pc * NPAIR + q + 1))
                    g.tensor_tensor(hl[:, p % 4, :], hb[:, p % 4, :], hh[:, p % 4, :].bitcast(F32),
                                    ALU.subtract).then_inc(S("hl"), 1)
                    if p == 1:
                        inverse_deviation(S, c + 1, CT)
                    if p == 6:
                        prep_low(S, c + 1)

            pool.wait_ge(A("xnew"), B - 1)
            g.memset(self32[:, :, :], 0.0).then_inc(cs("sel0"), 1)
            g.memset(zero[:, :], 0.0).then_inc(cs("zero"), 1)
            g.memset(gs[:, :, NGRP:], -9.0).then_inc(cs("sel1"), 1)
            g.memset(gr[:, :, TOPG:], -9.0).then_inc(cs("sel1"), 1)
            pool.wait_ge(cs("sel0"), 1)
            sel_v = self32[:, :, :].rearrange("k s (m i) -> k s m i", m=2)
            for part in range(2):
                g.affine_select(out=sel_v, in_=sel_v, compare_op=ALU.not_equal, fill=1.0, base=-part * E,
                                pattern=[[-2, SH], [-1, 2], [0, I]], channel_multiplier=1).then_inc(cs("sel2"), 1)
                pool.wait_ge(cs("sel2"), part + 1)
            inverse_deviation(F1, 0, CT)
            prep_low(F1, 0)
            experts(F1, 0)
            with pool.Fori(1, NC) as c:
                experts(F1, c)

            def keep_tiles(i):
                pool.wait_ge(M("xn"), CT * (i + 1))
                g.tensor_copy(xnb[:, ds(i * CH, CH)], xn[:, :, :].rearrange("p t d -> p (t d)")).then_inc(M("xb"), 1)

            inverse_deviation(M, 0, CT)
            keep_tiles(0)
            with pool.Fori(1, NC + 1) as c:
                inverse_deviation(M, c, CT)
                keep_tiles(c)
            inverse_deviation(F2, 0, CT)
            prep_low(F2, 0)
            experts(F2, 0)
            with pool.Fori(1, NC) as c:
                experts(F2, c)

        @block.scalar
        def _(act):
            s = nc.scalar
            act.wait_ge(ld("wa"), 16)
            s.activation(wah[:, :], wa[:, :], ACT.Copy).then_inc(cs("wah"), 1)

            def prep_high(b):
                act.wait_ge(A("xT"), b + 1)
                s.activation(xTh[:, :], PS[:, 0, 0:L], ACT.Copy).then_inc(A("xh"), 1)

            def keep_outputs(b, f):
                act.wait_ge(A("OT"), 4 * b + f + 1)
                s.activation(OTs[:, 2 * f:2 * f + 2, :], PS[:, 7, :].rearrange("p (k l) -> p k l", k=2),
                             ACT.Copy).then_inc(A("OTs"), 1)

            def keep_y(b, bank=0):
                act.wait_ge(A("y"), b + 1)
                s.activation(yTs[:, :], PS[:, bank, 0:L], ACT.Copy).then_inc(A("ys"), 1)

            def square_outputs(b, hf):
                act.wait_ge(A("av"), H * b + (hf + 1) * H // 2)
                after(act, A("n2o"), 2 * b + hf)
                s.activation(sqO[:, :, :], PS[:, 3 + 2 * hf:5 + 2 * hf, :], ACT.Square).then_inc(A("sqO"), 1)

            def tanh_norms(b, hf):
                act.wait_ge(A("n"), 2 * b + hf + 1)
                s.activation(th[:, :, :], nn[:, :, :], ACT.Tanh).then_inc(A("th"), 1)

            def attention(b, first):
                for t in range(2):
                    vbank = (1, 3)[t]
                    act.wait_ge(A("tv"), 2 * b + t + 1)
                    after(act, A("n2"), 4 * (b - 1) + 2 * t + 2)
                    s.activation(sq[:, t, 2 * QK:].rearrange("p (k n) -> p k n", k=2), PS[:, vbank:vbank + 2, :],
                                 ACT.Square).then_inc(A("sqv"), 1)
                    after(act, A("v"), 2 * (b - 1) + t + 1)
                    s.activation(vraw[:, t, :].rearrange("p (k n) -> p k n", k=2), PS[:, vbank:vbank + 2, :],
                                 ACT.Copy).then_inc(A("vraw"), 1)
                    act.wait_ge(A("tqk"), 2 * b + t + 1)
                    s.activation(sq[:, t, 0:2 * QK], PS[:, (3, 1)[t], :], ACT.Square).then_inc(A("sqqk"), 1)
                for gi in range(NG):
                    if not first and gi in (0, 2):
                        keep_outputs(b - 1, 2 + gi // 2)
                    act.wait_ge(A("qk"), NG * b + gi + 1)
                    s.activation(qkh[:, gi, :], PS[:, GBANK[gi], :], ACT.Copy).then_inc(A("qkh"), 1)
                for h in range(H):
                    act.wait_ge(A("S"), H * b + h + 1)
                    after(act, A("a"), H * b + h - 1)
                    s.activation(rl[:, h % 2, :], PS[:, 2 - h % 2, :], ACT.Relu).then_inc(A("relu"), 1)
                    if h == 1 and not first:
                        keep_y(b - 1)
                    if h == 8:
                        prep_high(b + 1)
                    if h == 9:
                        square_outputs(b, 0)
                    if h == 11:
                        tanh_norms(b, 0)
                keep_outputs(b, 0)
                keep_outputs(b, 1)
                square_outputs(b, 1)
                tanh_norms(b, 1)

            prep_high(0)
            attention(0, True)
            with act.Fori(1, B) as b:
                attention(b, False)

            def prep_chunk(S, i):
                act.wait_ge(*S.count("xT", i + 1))
                after(act, *S.count("lg", i))
                after(act, *S.count("xl", i))
                s.activation(x32[:, :], PS[:, 0, :], ACT.Copy).then_inc(S("x32"), 1)
                s.activation(fxh[:, ds(i * CH, CH)], PS[:, 0, :], ACT.Copy).then_inc(S("xh"), 1)

            def scores(S, i):
                act.wait_ge(*S.count("lg", i + 1))
                s.activation(sc[:, :], PS[:, 0, 0:CT * E], ACT.Sigmoid).then_inc(S("sc"), 1)

            def weights_high(S, i):
                act.wait_ge(*S.count("cT", i + 1))
                s.activation(wh[:, :], PS[0:2 * E, 0, :], ACT.Copy).then_inc(S("wh"), 1)

            def hidden_high(S, c, p):
                act.wait_ge(*S.count("h", c * NPAIR + p + 1))
                pc, q = prev(c, p, 4)
                after(act, *S.count("dn", pc * NPAIR + q + 1))
                s.activation(hh[:, p % 4, :], hb[:, p % 4, :], ACT.Copy).then_inc(S("hh"), 1)

            def keep_out(S, c):
                act.wait_ge(*S.count("dn", NPAIR * (c + 1)))
                s.activation(oT[:, :], PS[:, 7, :], ACT.Copy).then_inc(S("oT"), 1)

            def experts(S, c, first):
                for p in range(NPAIR):
                    act.wait_ge(*S.count("G", c * NPAIR + p + 1))
                    pc, q = prev(c, p, 2)
                    if q == SH:
                        after(act, *S.count("h", (pc + 1) * NPAIR))
                    else:
                        after(act, *S.count("t", pc * SH + q + 1))
                    s.activation(silu[:, p % 2, :], PS[:, 1 + p % 2, :], ACT.Silu).then_inc(S("silu"), 1)
                    if p:
                        hidden_high(S, c, p - 1)
                    elif not first:
                        hidden_high(S, c - 1, SH)
                    if p == 2 and not first:
                        keep_out(S, c - 1)
                    if p == 7:
                        prep_chunk(S, c + 1)
                    if p == 9:
                        scores(S, c + 1)
                    if p == 15:
                        weights_high(S, c + 1)

            def ffn(S):
                experts(S, 0, True)
                with act.Fori(1, NC) as c:
                    experts(S, c, False)

            def ffn_end(S):
                hidden_high(S, NC - 1, SH)
                keep_out(S, NC - 1)

            keep_outputs(B - 1, 2)
            keep_outputs(B - 1, 3)
            prep_chunk(F1, 0)
            keep_y(B - 1, 1)
            act.wait_ge(cs("sel2"), 2)
            s.activation(selr[:, :, :], self32[:, :, :], ACT.Copy).then_inc(cs("sel"), 1)
            scores(F1, 0)
            weights_high(F1, 0)
            ffn(F1)

            def mix_prep(i):
                act.wait_ge(M("xT"), i + 1)
                after(act, M("lg"), i)
                s.activation(x32[:, :], PS[:, 1, :], ACT.Copy).then_inc(M("x32"), 1)

            def mix_exp(c):
                act.wait_ge(M("ls"), c + 1)
                s.activation(ee[:, :, :], ls[:, :, :], ACT.Exp).then_inc(M("e"), 1)

            def mix_band(c):
                act.wait_ge(M("bT"), c + 1)
                after(act, M("o"), c)
                s.activation(bs1[:, :, :], PS[:, 3, :].rearrange("p (t l) -> p t l", t=CT), ACT.Copy).then_inc(M("bs1"), 1)

            ffn_end(F1)
            mix_prep(0)
            with act.Fori(0, NC) as c:
                mix_exp(c)
                mix_prep(c + 1)
            mix_band(0)
            with act.Fori(1, NC) as c:
                mix_band(c)
            prep_chunk(F2, 0)
            scores(F2, 0)
            weights_high(F2, 0)
            ffn(F2)
            ffn_end(F2)

        @block.vector
        def _(dve):
            v = nc.vector
            dve.wait_ge(cs("rid"), 1)
            v.tensor_scalar(rowbit[:, :], rowid[:, :], DK, None, ALU.bitwise_and).then_inc(cs("rbit"), 1)
            dve.wait_ge(cs("rbit"), 1)
            v.tensor_scalar(lowrows[:, :], rowbit[:, :], -1.0 / DK, None, ALU.mult).then_inc(cs("low"), 1)

            def tile_stats(S, i, n):
                for t in range(n):
                    v.bn_stats(stats[:, t, :], Xt(i * n + t)).then_inc(S("stats"), 1)
                after(dve, *S.count("rstd", i))
                wait_apart(dve, cs("rbit"), *S.count("stats", n * (i + 1)))
                for t in range(n):
                    v.bn_aggr(mv[:, t, :], stats[:, t, :]).then_inc(S("mv"), 1)

            def normalise(S, i, n):
                dve.wait_ge(*S.count("rstd", i + 1))
                dve.wait_ge(*S.count("mv", n * (i + 1)))
                after(dve, *S.count("xT", i))
                for t in range(n):
                    v.tensor_scalar(xn[:, t, :], Xt(i * n + t), mv[:, t, 0:1], rstd[:, t:t + 1],
                                    ALU.subtract, ALU.mult).then_inc(S("xn"), 1)

            def prep_low(b):
                dve.wait_ge(A("xh"), b + 1)
                v.tensor_tensor(xTl[:, :], PS[:, 0, 0:L], xTh[:, :].bitcast(F32), ALU.subtract).then_inc(A("xl"), 1)

            def scale_outputs(b, hf):
                k = 2 * b + hf + 1
                hs = slice(hf * (H // 2), (hf + 1) * (H // 2))
                dve.wait_ge(A("sqO"), k)
                after(dve, A("sr"), k - 1)
                v.tensor_reduce(n2o[:, :, :], sqO[:, :, :].rearrange("p i (h d) -> p i h d", d=DV), AX.X,
                                ALU.add).then_inc(A("n2o"), 1)
                return k, hs

            def scale_outputs_end(b, hf, k, hs):
                dve.wait_ge(A("n"), k)
                v.tensor_scalar(nmx[:, :, :], nn[:, :, :], NORM_EPS, None, ALU.max).then_inc(A("nmx"), 1)
                dve.wait_ge(A("nmx"), k)
                v.reciprocal(rec[:, :, :], nmx[:, :, :]).then_inc(A("rec"), 1)
                dve.wait_ge(A("rec"), k)
                v.tensor_tensor(f1[:, :, :], rec[:, :, :], rr[:, :, hs], ALU.mult).then_inc(A("f1"), 1)
                dve.wait_ge(A("f1"), k)
                dve.wait_ge(A("th"), k)
                v.tensor_tensor(ff[:, :, :], f1[:, :, :], th[:, :, :], ALU.mult).then_inc(A("f"), 1)
                dve.wait_ge(A("f"), k)
                after(dve, A("OT"), 4 * (b - 1) + 2 * hf + 2)
                v.tensor_tensor(Op[:, hf, :, :].rearrange("p i (h d) -> p i h d", d=DV),
                                PS[:, 3 + 2 * hf:5 + 2 * hf, :].rearrange("p i (h d) -> p i h d", d=DV),
                                ff[:, :, :].unsqueeze(3).to_broadcast([P, 2, H // 2, DV]), ALU.mult).then_inc(A("op"), 1)

            def add_attention(b, bank=0):
                dve.wait_ge(A("yT"), b + 1)
                v.tensor_tensor(Xt(2 * b, 2), Xt(2 * b, 2), PS[:, bank, L:2 * L], ALU.add).then_inc(A("xnew"), 1)

            def attention(b, first):
                for t in range(2):
                    dve.wait_ge(A("sqv"), 2 * b + t + 1)
                    v.tensor_reduce(n2[:, t, 2 * H:3 * H], sq[:, t, 2 * QK:].rearrange("p (h d) -> p h d", d=DV),
                                    AX.X, ALU.add).then_inc(A("n2"), 1)
                    dve.wait_ge(A("sqqk"), 2 * b + t + 1)
                    v.tensor_reduce(n2[:, t, 0:2 * H], sq[:, t, 0:2 * QK].rearrange("p (h d) -> p h d", d=DK),
                                    AX.X, ALU.add).then_inc(A("n2"), 1)
                dve.wait_ge(A("n2"), 4 * b + 4)
                after(dve, A("v"), 2 * b)
                v.tensor_scalar(nm[:, :, :], n2[:, :, :], NORM_EPS * NORM_EPS, None, ALU.max).then_inc(A("nm"), 1)
                dve.wait_ge(A("nm"), b + 1)
                after(dve, A("n"), 2 * b)
                v.reciprocal(rr[:, :, :], nm[:, :, 0:2 * H]).then_inc(A("rr"), 1)
                for gi in range(NG):
                    dve.wait_ge(A("qkh"), NG * b + gi + 1)
                    bank = GBANK[gi]
                    v.tensor_tensor(ql[:, gi, :], PS[:, bank, 0:L], qkh[:, gi, 0:L].bitcast(F32),
                                    ALU.subtract).then_inc(A("kql"), 1)
                    v.scalar_tensor_tensor(kst[:, gi, :], qkh[:, gi, L:2 * L].bitcast(F32), lowrows[:, 0:1],
                                           PS[:, bank, L:2 * L], ALU.mult, ALU.add).then_inc(A("kql"), 1)
                for h in range(H):
                    dve.wait_ge(A("relu"), H * b + h + 1)
                    after(dve, A("av"), H * b + h - 3)
                    v.scalar_tensor_tensor(aT[:, h % 4, :], PS[:, 2 - h % 2, :], 0.0, rl[:, h % 2, :],
                                           ALU.max, ALU.mult).then_inc(A("a"), 1)
                    if h == 2 and not first:
                        add_attention(b - 1)
                    if h == 3:
                        if first:
                            dve.wait_ge(ld("x"), 16)
                            dve.wait_ge(cs("pad"), 1)
                        tile_stats(A, b + 1, 2)
                    if h == 5:
                        normalise(A, b + 1, 2)
                    if h == 8:
                        prep_low(b + 1)
                    if h == 10:
                        mid = scale_outputs(b, 0)
                    if h == 12:
                        scale_outputs_end(b, 0, *mid)
                scale_outputs_end(b, 1, *scale_outputs(b, 1))

            v.memset(wf[I:P, WD0 + SH * P:WF], 0.0).then_inc(cs("dpad"), 1)
            v.memset(negw[0:E, :], 0.0).then_inc(cs("neg"), 1)
            v.memset(negw[E:2 * E, :], -1.0).then_inc(cs("neg"), 1)
            dve.wait_ge(ld("x0"), 16)
            tile_stats(A, 0, 2)
            normalise(A, 0, 2)
            dve.wait_ge(cs("wah"), 1)
            v.tensor_tensor(wal[:, :], wa[:, :], wah[:, :].bitcast(F32), ALU.subtract).then_inc(cs("wal"), 1)
            prep_low(0)
            dve.wait_ge(cs("low"), 1)
            attention(0, True)
            with dve.Fori(1, B) as b:
                attention(b, False)

            def group_scores(S, i):
                dve.wait_ge(*S.count("sc", i + 1))
                v.tensor_reduce(gs[:, :, 0:NGRP], sc[:, :].rearrange("p (t g e) -> p t g e", t=CT, e=EPG), AX.X,
                                ALU.add).then_inc(S("gs"), 1)
                wait_apart(dve, cs("rbit"), *S.count("gs", i + 1))
                for t in range(CT):
                    v.max(g8[:, t, :], gs[:, t, 0:NGRP]).then_inc(S("g8"), 1)

            def choose_groups(S, i):
                dve.wait_ge(*S.count("g8", CT * (i + 1)))
                v.tensor_copy(gr[:, :, 0:TOPG], g8[:, :, 0:TOPG]).then_inc(S("gr"), 1)
                wait_apart(dve, cs("rbit"), *S.count("gr", i + 1))
                for t in range(CT):
                    v.match_replace(gm[:, t, :], gr[:, t, :], gs[:, t, :], -1.0).then_inc(S("gm"), 1)

            def mask_scores(S, i):
                dve.wait_ge(*S.count("gm", CT * (i + 1)))
                v.tensor_scalar(gsel[:, :].rearrange("p (t g) -> p t g", t=CT), gm[:, :, 0:NGRP], 0.0, None,
                                ALU.is_lt).then_inc(S("gsel"), 1)
                dve.wait_ge(*S.count("gsel", i + 1))
                v.tensor_tensor(ms[:, :, :].rearrange("p t (g e) -> p (t g) e", e=EPG),
                                sc[:, :].rearrange("p (g e) -> p g e", e=EPG),
                                gsel[:, :].unsqueeze(2).to_broadcast([P, CT * NGRP, EPG]), ALU.mult).then_inc(S("ms"), 1)
                wait_apart(dve, cs("rbit"), *S.count("ms", i + 1))
                for t in range(CT):
                    v.max(m8[:, t, :], ms[:, t, :]).then_inc(S("m8"), 1)

            def choose_experts(S, i):
                wait_apart(dve, cs("rbit"), *S.count("m8", CT * (i + 1)))
                for t in range(CT):
                    v.match_replace(mr[:, t, :], m8[:, t, :], ms[:, t, :], 0.0).then_inc(S("mr"), 1)
                v.tensor_reduce(ws[:, :], m8[:, :, :], AX.X, ALU.add).then_inc(S("ws"), 1)
                dve.wait_ge(*S.count("ws", i + 1))
                v.tensor_scalar(wmx[:, :], ws[:, :], 1e-12, None, ALU.max).then_inc(S("wmx"), 1)
                dve.wait_ge(*S.count("mr", CT * (i + 1)))
                v.tensor_tensor(wsel[:, :, :], ms[:, :, :], mr[:, :, :], ALU.subtract).then_inc(S("wsel"), 1)
                dve.wait_ge(*S.count("wmx", i + 1))
                v.reciprocal(winv[:, :], wmx[:, :]).then_inc(S("winv"), 1)
                dve.wait_ge(*S.count("winv", i + 1))
                dve.wait_ge(*S.count("wsel", i + 1))
                after(dve, *S.count("cT", i))
                for part in range(2):
                    v.tensor_tensor(comb[:, :, part, :], wsel[:, :, :],
                                    winv[:, :].unsqueeze(2).to_broadcast([P, CT, E]), ALU.mult).then_inc(S("comb"), 1)

            def weights_low(S, i):
                dve.wait_ge(*S.count("wh", i + 1))
                dve.wait_ge(cs("neg"), 2)
                v.scalar_tensor_tensor(wT[:, ds(i * CH, CH)], wh[:, :].bitcast(F32), negw[:, 0:1],
                                       PS[0:2 * E, 0, :], ALU.mult, ALU.add).then_inc(S("wT"), 1)

            def route(S, i):
                group_scores(S, i)
                choose_groups(S, i)
                mask_scores(S, i)
                choose_experts(S, i)

            def weighted(S, c, p):
                n = c * NPAIR + p
                dve.wait_ge(*S.count("WB", c * SH + p + 1))
                dve.wait_ge(*S.count("t", c * SH + p + 1))
                pc, q = prev(c, p, 4)
                after(dve, *S.count("hl", pc * NPAIR + q + 1))
                v.tensor_tensor(hb[:, p % 4, :], tt[:, p % 2, :], PS[:, 5 + p % 2, :], ALU.mult).then_inc(S("h"), 1)

            def add_experts(S, c):
                dve.wait_ge(*S.count("fin", c + 1))
                v.tensor_tensor(Xt(c * CT, CT), Xt(c * CT, CT), PS[:, 0, :], ALU.add).then_inc(S("xnew"), 1)

            def experts(S, c, first, x_ready):
                for p in range(NPAIR):
                    dve.wait_ge(*S.count("silu", c * NPAIR + p + 1))
                    dve.wait_ge(*S.count("U", c * NPAIR + p + 1))
                    if p < SH:
                        v.tensor_tensor(tt[:, p % 2, :], silu[:, p % 2, :], PS[:, 3 + p % 2, :],
                                        ALU.mult).then_inc(S("t"), 1)
                    if p:
                        weighted(S, c, p - 1)
                    if p == SH:
                        pc, q = prev(c, p, 4)
                        after(dve, *S.count("hl", pc * NPAIR + q + 1))
                        v.tensor_tensor(hb[:, p % 4, :], silu[:, p % 2, :], PS[:, 3 + p % 2, :],
                                        ALU.mult).then_inc(S("h"), 1)
                    if p == 1:
                        if first and x_ready:
                            dve.wait_ge(*x_ready)
                        tile_stats(S, c + 1, CT)
                    if p == 3:
                        normalise(S, c + 1, CT)
                    if p == 5 and not first:
                        add_experts(S, c - 1)
                    if p == 10:
                        group_scores(S, c + 1)
                    if p == 11:
                        choose_groups(S, c + 1)
                    if p == 12:
                        mask_scores(S, c + 1)
                    if p == 13:
                        choose_experts(S, c + 1)
                    if p == 16:
                        weights_low(S, c + 1)

            def ffn(S, x_ready):
                experts(S, 0, True, x_ready)
                with dve.Fori(1, NC) as c:
                    experts(S, c, False, x_ready)

            tile_stats(F1, 0, CT)
            normalise(F1, 0, CT)
            add_attention(B - 1, 1)
            dve.wait_ge(cs("sel1"), 2)
            route(F1, 0)
            weights_low(F1, 0)
            ffn(F1, (A("xnew"), B))

            def taps(c):
                dve.wait_ge(M("lg"), c + 1)
                v.tensor_tensor(lb[:, :, :], PS[:, 2, 0:CT * K].rearrange("p (t k) -> p t k", t=CT),
                                bb[:, :].unsqueeze(1).to_broadcast([P, CT, K]), ALU.add).then_inc(M("lb"), 1)
                dve.wait_ge(M("lb"), c + 1)
                v.tensor_reduce(mx[:, :], lb[:, :, :], AX.X, ALU.max).then_inc(M("mx"), 1)
                dve.wait_ge(M("mx"), c + 1)
                v.tensor_tensor(ls[:, :, :], lb[:, :, :], mx[:, :].unsqueeze(2).to_broadcast([P, CT, K]),
                                ALU.subtract).then_inc(M("ls"), 1)
                tile_stats(M, c + 1, CT)
                dve.wait_ge(M("e"), c + 1)
                v.tensor_reduce(es[:, :], ee[:, :, :], AX.X, ALU.add).then_inc(M("es"), 1)
                dve.wait_ge(M("es"), c + 1)
                v.reciprocal(er[:, :], es[:, :]).then_inc(M("er"), 1)
                dve.wait_ge(M("er"), c + 1)
                v.tensor_tensor(wS[:, ds(c * CT * K, CT * K)].rearrange("p (t k) -> p t k", t=CT), ee[:, :, :],
                                er[:, :].unsqueeze(2).to_broadcast([P, CT, K]), ALU.mult).then_inc(M("w"), 1)
                after(dve, M("xb"), c + 1)
                normalise(M, c + 1, CT)

            def add_mix(c):
                dve.wait_ge(M("bT"), c + 1)
                v.tensor_copy(bs2[:, :, :], PS[0:K, 4, 0:CT // 2 * P].rearrange("p (t l) -> p t l", l=P)).then_inc(M("bs2"), 1)
                dve.wait_ge(M("o"), c + 1)
                v.tensor_tensor(Xt(c * CT, CT), Xt(c * CT, CT), PS[:, 5, :], ALU.add).then_inc(M("xnew"), 1)

            dve.wait_ge(*F1.count("xnew", 1))
            tile_stats(M, 0, CT)
            normalise(M, 0, CT)
            add_experts(F1, NC - 1)
            dve.wait_ge(*F1.count("xnew", NC))
            dve.wait_ge(ld("bb"), 16)
            with dve.Fori(0, NC) as c:
                taps(c)
            with dve.Fori(0, NC) as c:
                add_mix(c)
            dve.wait_ge(M("xnew"), NC)
            tile_stats(F2, 0, CT)
            normalise(F2, 0, CT)
            route(F2, 0)
            weights_low(F2, 0)
            ffn(F2, None)
            add_experts(F2, NC - 1)

        @block.tensor
        def _(pe):
            def mm(o, w, m, start, stop):
                return nc.tensor.matmul(o, w, m, start=start, stop=stop)

            def split3(o, wh_, wl_, mh_, ml_, start=True, stop=True):
                mm(o, wh_, mh_, start, False)
                mm(o, wh_, ml_, False, False)
                return mm(o, wl_, mh_, False, stop)

            def transpose_x(S, i, n, bank):
                pe.wait_ge(*S.count("xn", n * (i + 1)))
                for t in range(n):
                    last = nc.tensor.transpose(PS[:, bank, t * P:(t + 1) * P], xn[:, t, :], ident[:, :])
                last.then_inc(S("xT"), 1)

            def by_token(t, w0, bank):
                cols = slice(t * P, (t + 1) * P)
                return split3(PS[:, bank, :], xTh[:, cols], xTl[:, cols], wah[:, w0:w0 + 512], wal[:, w0:w0 + 512])

            def qk_group(b, gi):
                bank = GBANK[gi]
                for part, w0 in enumerate((WQ_G, WK_G)):
                    cols = slice(w0 + gi * P, w0 + (gi + 1) * P)
                    last = split3(PS[:, bank, part * L:(part + 1) * L], wah[:, cols], wal[:, cols], xTh[:, :], xTl[:, :])
                last.then_inc(A("qk"), 1)

            def score(b, h):
                gi, rows = h // HG, slice(SLOT * (h % HG), SLOT * (h % HG + 1))
                pe.wait_ge(A("kql"), 2 * NG * b + (2 if h == 0 else 2 * NG))
                after(pe, A("a"), H * b + h - 1)
                for jt in range(2):
                    o = PS[:, 2 - h % 2, jt * L:(jt + 1) * L]
                    keys = kst[rows, gi, jt * P:(jt + 1) * P]
                    mm(o, keys, qkh[rows, gi, 0:L], True, False)
                    last = mm(o, keys, ql[rows, gi, :], False, True)
                last.then_inc(A("S"), 1)

            def attend(b, h):
                pe.wait_ge(A("a"), H * b + h + 1)
                hf, col = h // (H // 2), (h % (H // 2)) * DV
                if h == H // 2:
                    after(pe, A("op"), 2 * b)
                for it in range(2):
                    for jt in range(2):
                        last = mm(PS[:, 3 + 2 * hf + it, col:col + DV], aT[:, h % 4, jt * L + it * P:jt * L + (it + 1) * P],
                                  vp[:, jt, h * DV:(h + 1) * DV], jt == 0, jt == 1)
                last.then_inc(A("av"), 1)

            def transpose_outputs(b, f):
                hf = f // 2
                pe.wait_ge(A("op"), 2 * b + hf + 1)
                after(pe, A("OTs"), 4 * b + f)
                for k in range(2):
                    cols = slice((2 * (f % 2) + k) * P, (2 * (f % 2) + k + 1) * P)
                    for it in range(2):
                        last = nc.tensor.transpose(PS[:, 7, k * L + it * P:k * L + (it + 1) * P], Op[:, hf, it, cols],
                                                   ident[:, :])
                last.then_inc(A("OT"), 1)

            def project(b, bank=0):
                pe.wait_ge(A("OTs"), 4 * (b + 1))
                nk = H * DV // P
                for k in range(nk):
                    last = mm(PS[:, bank, 0:L], wout[:, k, :], OTs[:, k, :], k == 0, k == nk - 1)
                last.then_inc(A("y"), 1)

            def transpose_y(b, bank=0):
                pe.wait_ge(A("ys"), b + 1)
                for t in range(2):
                    last = nc.tensor.transpose(PS[:, bank, L + t * P:L + (t + 1) * P], yTs[:, t * P:(t + 1) * P],
                                               ident[:, :])
                last.then_inc(A("yT"), 1)

            def attention(b, first):
                pe.wait_ge(A("xh"), b + 1)
                pe.wait_ge(A("xl"), b + 1)
                after(pe, A("a"), H * b)
                by_token(0, W_V, 1)
                by_token(0, W_V + 512, 2).then_inc(A("tv"), 1)
                after(pe, A("op"), 2 * b - 1)
                by_token(0, W_QK, 3).then_inc(A("tqk"), 1)
                pe.wait_ge(A("sqqk"), 2 * b + 1)
                by_token(1, W_V, 3)
                by_token(1, W_V + 512, 4).then_inc(A("tv"), 1)
                pe.wait_ge(A("vraw"), 2 * b + 1)
                by_token(1, W_QK, 1).then_inc(A("tqk"), 1)
                if not first:
                    transpose_outputs(b - 1, 2)
                qk_group(b, 0)
                pe.wait_ge(A("vraw"), 2 * b + 2)
                qk_group(b, 1)
                if not first:
                    transpose_outputs(b - 1, 3)
                qk_group(b, 2)
                pe.wait_ge(A("sqqk"), 2 * b + 2)
                qk_group(b, 3)
                score(b, 0)
                score(b, 1)
                if not first:
                    project(b - 1)
                pe.wait_ge(A("v"), 2 * b + 2)
                for h in range(H):
                    attend(b, h)
                    if h + 2 < H:
                        score(b, h + 2)
                    if h == 1 and not first:
                        transpose_y(b - 1)
                    if h == 6:
                        after(pe, A("xnew"), b)
                        transpose_x(A, b + 1, 2, 0)
                    if h == 13:
                        transpose_outputs(b, 0)
                    if h == 14:
                        transpose_outputs(b, 1)

            pe.wait_ge(cs("id"), 1)
            transpose_x(A, 0, 2, 0)
            pe.wait_ge(cs("wal"), 1)
            attention_first = True
            pe.wait_ge(ld("wo"), 16)
            attention(0, attention_first)
            with pe.Fori(1, B) as b:
                attention(b, False)

            def logits(S, i):
                pe.wait_ge(*S.count("x32", i + 1))
                pe.wait_ge(*S.count("xh", i + 1))
                for t in range(CT):
                    last = mm(PS[:, 0, t * E:(t + 1) * E], x32[:, t * P:(t + 1) * P], gw[:, :], True, True)
                last.then_inc(S("lg"), 1)

            def transpose_weights(S, i):
                wait_apart(pe, cs("id"), *S.count("comb", 2 * (i + 1)))
                for t in range(CT):
                    last = nc.tensor.transpose(PS[0:2 * E, 0, t * P:(t + 1) * P],
                                               comb[:, t, :, :].rearrange("p a e -> p (a e)"), ident[:, :])
                last.then_inc(S("cT"), 1)

            def down(S, c, p):
                n = c * NPAIR + p
                pe.wait_ge(*S.count("hl", n + 1))
                if p == 0:
                    after(pe, *S.count("oT", c))
                cols = slice(WD0 + p * P, WD0 + (p + 1) * P)
                split3(PS[:, 7, :], wfh[:, cols], wfl[:, cols], hh[:, p % 4, :], hl[:, p % 4, :],
                              start=p == 0, stop=p == SH).then_inc(S("dn"), 1)

            def transpose_out(S, c):
                pe.wait_ge(*S.count("oT", c + 1))
                pe.wait_ge(*S.count("wT", c + 1))
                for t in range(CT):
                    last = nc.tensor.transpose(PS[:, 0, t * P:(t + 1) * P], oT[:, t * P:(t + 1) * P], ident[:, :])
                last.then_inc(S("fin"), 1)

            def experts(S, c, first):
                xh_, xl_ = fxh[:, ds(c * CH, CH)], fxl[:, ds(c * CH, CH)]
                for p in range(NPAIR):
                    if p >= LAG:
                        down(S, c, p - LAG)
                    elif not first:
                        down(S, c - 1, NPAIR + p - LAG)
                    if p == 0:
                        pe.wait_ge(*S.count("xl", c + 1))
                        pe.wait_ge(*S.count("wT", c + 1))
                    pc, q = prev(c, p, 2)
                    gcols = slice(WG0 + p * P, WG0 + (p + 1) * P)
                    ucols = slice(WU0 + p * P, WU0 + (p + 1) * P)
                    after(pe, *S.count("silu", pc * NPAIR + q + 1))
                    split3(PS[:, 1 + p % 2, :], wfh[:, gcols], wfl[:, gcols], xh_, xl_).then_inc(S("G"), 1)
                    if q == SH:
                        after(pe, *S.count("h", (pc + 1) * NPAIR))
                    else:
                        after(pe, *S.count("t", pc * SH + q + 1))
                    split3(PS[:, 3 + p % 2, :], wfh[:, ucols], wfl[:, ucols], xh_, xl_).then_inc(S("U"), 1)
                    if p < SH:
                        wc, wq = (c, p - 2) if p >= 2 else (c - 1, SH - 2 + p)
                        wait_apart(pe, cs("id"), *S.count("h", wc * NPAIR + wq + 1))
                        mm(PS[:, 5 + p % 2, :], selr[:, p, :], wT[:, ds(c * CH, CH)], True, True).then_inc(S("WB"), 1)
                    if p == 4 and not first:
                        transpose_out(S, c - 1)
                    if p == 6:
                        after(pe, *S.count("xnew", c))
                        pe.wait_ge(*S.count("wT", c + 1))
                        transpose_x(S, c + 1, CT, 0)
                    if p == 8:
                        logits(S, c + 1)
                    if p == 15:
                        transpose_weights(S, c + 1)

            def ffn(S):
                experts(S, 0, True)
                with pe.Fori(1, NC) as c:
                    experts(S, c, False)

            def ffn_end(S):
                for p in range(NPAIR - LAG, NPAIR):
                    down(S, NC - 1, p)
                pe.wait_ge(*S.count("wT", NC + 1))
                transpose_out(S, NC - 1)

            transpose_outputs(B - 1, 2)
            transpose_outputs(B - 1, 3)
            pe.wait_ge(A("xl"), B + 1)
            transpose_x(F1, 0, CT, 0)
            project(B - 1, 1)
            pe.wait_ge(ld("gw"), 16)
            logits(F1, 0)
            transpose_y(B - 1, 1)
            transpose_weights(F1, 0)
            pe.wait_ge(A("xnew"), B)
            pe.wait_ge(cs("wf"), 2 * B)
            pe.wait_ge(cs("sel"), 1)
            ffn(F1)

            def taps_logits(c):
                pe.wait_ge(M("x32"), c + 1)
                after(pe, M("lb"), c)
                for t in range(CT):
                    last = mm(PS[:, 2, t * K:(t + 1) * K], x32[:, t * P:(t + 1) * P], wb[:, :], True, True)
                last.then_inc(M("lg"), 1)

            def mix(c, first):
                pe.wait_ge(M("get"), 16 * (c + 1))
                after(pe, M("bs1"), c)
                after(pe, M("bs2"), c)
                for t in range(CT):
                    nc.tensor.transpose(PS[:, 3, t * P:(t + 1) * P], band4[:, t, 0:P], ident[:, :])
                for j in range(CT // 2):
                    last = nc.tensor.transpose(PS[0:K, 4, j * P:(j + 1) * P], band4[:, 2 * j, P:BW], ident[:, :])
                last.then_inc(M("bT"), 1)
                pe.wait_ge(M("bs1"), c + 1)
                pe.wait_ge(M("bs2"), c + 1)
                after(pe, M("xnew"), c)
                for t in range(CT):
                    o = PS[:, 5, t * P:(t + 1) * P]
                    last = mm(o, bs1[:, t, :], xnb[:, ds((c * CT + t) * P, P)], True, t % 2 == 1)
                    if t % 2 == 0:
                        last = mm(o, bs2[:, t // 2, :], xnb[0:K, ds((c * CT + t + 1) * P, P)], False, True)
                last.then_inc(M("o"), 1)

            pe.wait_ge(*F1.count("h", NC * NPAIR))
            ffn_end(F1)
            transpose_x(M, 0, CT, 1)
            pe.wait_ge(ld("wb"), 16)
            taps_logits(0)
            transpose_x(M, 1, CT, 1)
            with pe.Fori(1, NC) as c:
                taps_logits(c)
                transpose_x(M, c + 1, CT, 1)
            pe.wait_ge(M("xb"), NC + 1)
            mix(0, True)
            with pe.Fori(1, NC) as c:
                mix(c, False)
            transpose_x(F2, 0, CT, 0)
            logits(F2, 0)
            transpose_weights(F2, 0)
            ffn(F2)
            ffn_end(F2)


INPUTS = ["x", "wa", "wo", "wb", "bb", "gw", "eg", "eu", "ed", "sg", "su", "sd"]


def layout(L0_attn_a_tokens, L0_attn_a_Wq, L0_attn_a_Wkv, L0_attn_a_Wout, L0_attn_b_W, L0_attn_b_b, L0_ffn_gate_w,
           L0_ffn_expert_gate, L0_ffn_expert_up, L0_ffn_expert_down, L0_ffn_shared_gate_w, L0_ffn_shared_up_w,
           L0_ffn_shared_down_w):
    def c(a):
        return np.ascontiguousarray(a)

    wq = np.asarray(L0_attn_a_Wq)
    wkv = np.asarray(L0_attn_a_Wkv).reshape(D, H, DK + DV)
    wk, wv = wkv[:, :, :DK], wkv[:, :, DK:]
    q_twice = np.stack([wq.reshape(D, H, DK)] * 2, axis=2).reshape(D, H * SLOT)
    k_twice = np.stack([wk] * 2, axis=2).reshape(D, H * SLOT)
    wa = np.concatenate([q_twice, k_twice, wq, wk.reshape(D, H * DK), wv.reshape(D, H * DV)], axis=1)
    ed = np.asarray(L0_ffn_expert_down).reshape(SH, 2, D, I).transpose(1, 3, 0, 2).reshape(2 * I, SH * D)
    return {
        "x": c(np.asarray(L0_attn_a_tokens).reshape(T, D)),
        "wa": c(wa),
        "wo": c(np.asarray(L0_attn_a_Wout)),
        "wb": c(np.asarray(L0_attn_b_W).T),
        "bb": c(np.asarray(L0_attn_b_b)),
        "gw": c(np.asarray(L0_ffn_gate_w).T),
        "eg": c(np.asarray(L0_ffn_expert_gate).transpose(2, 0, 1).reshape(D, E * I)),
        "eu": c(np.asarray(L0_ffn_expert_up).transpose(2, 0, 1).reshape(D, E * I)),
        "ed": c(ed),
        "sg": c(np.asarray(L0_ffn_shared_gate_w).T),
        "su": c(np.asarray(L0_ffn_shared_up_w).T),
        "sd": c(np.asarray(L0_ffn_shared_down_w).T),
    }


def kernel(**inputs):
    import concourse.bacc as bacc
    from concourse.bass_utils import run_bass_kernel_spmd

    arrays = layout(**inputs)
    nc = bacc.Bacc("TRN2", target_bir_lowering=False, num_devices=1)
    args = [nc.dram_tensor(f"{n}_dram", arrays[n].shape, mybir.dt.from_np(arrays[n].dtype), kind="ExternalInput").ap()
            for n in INPUTS]
    band = nc.dram_tensor("band_dram", (NT, P * (BW + 1)), F32, kind="Internal").ap()
    out = nc.dram_tensor("out_dram", (T, D), F32, kind="ExternalOutput").ap()
    hybrid_layer(nc, *args, band, out)
    r = run_bass_kernel_spmd(nc, [{f"{n}_dram": arrays[n] for n in INPUTS}], core_ids=[0])
    return r.results[0]["out_dram"].reshape(B, L, D)
```
